# Optimizing a Trainium2 kernel written in Bass

```python
import numpy as np
import jax
import jax.numpy as jnp

def _softmax(x, axis=-1):
    return jax.nn.softmax(x, axis=axis)

def _gelu(x):
    return jax.nn.gelu(x, approximate=True)

def _silu(x):
    return jax.nn.silu(x)

def _sigmoid(x):
    return jax.nn.sigmoid(x)

def _layernorm(x, axis=-1, eps=1e-05):
    m = jnp.mean(x, axis=axis, keepdims=True)
    v = jnp.var(x, axis=axis, keepdims=True)
    return (x - m) / jnp.sqrt(v + eps)

def _scatter_add(tgt, idx, src, axis=0):
    return tgt.at[idx].add(src)

def _segment_sum(src, seg, n):
    return jax.ops.segment_sum(src, seg, n)
kernel_name = 'mk_seq_postln_d1_jaxref_r2_f03249'

def setup_inputs(seed: int=0):
    np.random.seed(seed)
    _w = jnp.asarray

    def _L0_attn_setup():
        import jax, jax.numpy as jnp
        import numpy as np
        B, L, H, U = (4, 2048, 512, 512)
        key = jax.random.key(seed)
        k0, k1, k2, k3 = jax.random.split(key, 4)
        inputs = jax.random.normal(k0, (B, L, H), dtype=jnp.float32)
        W_rkv = jax.random.normal(k1, (H, 3 * U), dtype=jnp.float32) / np.sqrt(H)
        b_rkv = jnp.zeros((3 * U,), dtype=jnp.float32)
        W_o = jax.random.normal(k2, (U, H), dtype=jnp.float32) / np.sqrt(U)
        b_o = jnp.zeros((H,), dtype=jnp.float32)
        r_min, r_max = (0.9, 0.999)
        u = jax.random.uniform(k3, (U,), dtype=jnp.float32)
        nu_log = jnp.log(-0.5 * jnp.log(u * (r_max ** 2 - r_min ** 2) + r_min ** 2))
        gamma_log = jnp.zeros((U,), dtype=jnp.float32)
        return {'inputs': inputs, 'W_rkv': W_rkv, 'b_rkv': b_rkv, 'W_o': W_o, 'b_o': b_o, 'nu_log': nu_log, 'gamma_log': gamma_log}
    _L0_attn_in = _L0_attn_setup()

    def _L0_ffn_setup():
        import jax, jax.numpy as jnp
        import numpy as np
        DIM = 512

        def _reference_tuple_inner(x, W_r, W_k, W_v, mu_r, mu_k):
            B, T, C = x.shape
            x_prev = jnp.concatenate([jnp.zeros((B, 1, C), x.dtype), x[:, :-1, :]], axis=1)
            xr = mu_r * x + (1.0 - mu_r) * x_prev
            xk = mu_k * x + (1.0 - mu_k) * x_prev
            r = jax.nn.sigmoid(jnp.einsum('btc,dc->btd', xr, W_r))
            k = jnp.einsum('btc,dc->btd', xk, W_k)
            k_act = jnp.square(jax.nn.relu(k))
            out = r * jnp.einsum('btc,dc->btd', k_act, W_v)
            new_state = x[:, -1, :]
            return (out, new_state)
        key = jax.random.key(seed)
        ks = jax.random.split(key, 6)
        B, T, C = (8, 1024, DIM)
        x = jax.random.normal(ks[0], (B, T, C), dtype=jnp.float32)
        s = 1.0 / np.sqrt(C)
        W_r = jax.random.uniform(ks[1], (C, C), jnp.float32, -s, s)
        W_k = jax.random.uniform(ks[2], (C, C), jnp.float32, -s, s)
        W_v = jax.random.uniform(ks[3], (C, C), jnp.float32, -s, s)
        mu_r = jax.random.uniform(ks[4], (C,), jnp.float32)
        mu_k = jax.random.uniform(ks[5], (C,), jnp.float32)
        return {'x': x, 'W_r': W_r, 'W_k': W_k, 'W_v': W_v, 'mu_r': mu_r, 'mu_k': mu_k}
    _L0_ffn_in = _L0_ffn_setup()
    _d = {'L0_attn_inputs': _L0_attn_in['inputs'], 'L0_attn_W_rkv': _L0_attn_in['W_rkv'], 'L0_attn_b_rkv': _L0_attn_in['b_rkv'], 'L0_attn_W_o': _L0_attn_in['W_o'], 'L0_attn_b_o': _L0_attn_in['b_o'], 'L0_attn_nu_log': _L0_attn_in['nu_log'], 'L0_attn_gamma_log': _L0_attn_in['gamma_log'], 'L0_ffn_W_r': _L0_ffn_in['W_r'], 'L0_ffn_W_k': _L0_ffn_in['W_k'], 'L0_ffn_W_v': _L0_ffn_in['W_v'], 'L0_ffn_mu_r': _L0_ffn_in['mu_r'], 'L0_ffn_mu_k': _L0_ffn_in['mu_k']}
    _x0 = _d['L0_attn_inputs']
    _d['L0_attn_inputs'] = jax.random.normal(jax.random.fold_in(jax.random.key(seed), 1), (8, 2048, 512), dtype=_x0.dtype)
    del _x0
    return _d

def reference(L0_attn_inputs, L0_attn_W_rkv, L0_attn_b_rkv, L0_attn_W_o, L0_attn_b_o, L0_attn_nu_log, L0_attn_gamma_log, L0_ffn_W_r, L0_ffn_W_k, L0_ffn_W_v, L0_ffn_mu_r, L0_ffn_mu_k):

    def _L0_attn_ref(inputs, W_rkv, b_rkv, W_o, b_o, nu_log, gamma_log):
        import jax, jax.numpy as jnp
        import numpy as np
        B, L, H, U = (4, 2048, 512, 512)
        rkv = jnp.einsum('blh,hu->blu', inputs, W_rkv) + b_rkv
        r, k, v = jnp.split(rkv, 3, axis=-1)
        r = jax.nn.sigmoid(r)
        k = jnp.exp(k)
        kv = k * v
        u = jnp.concatenate([kv, k], axis=-1)
        nu = jnp.exp(jnp.concatenate([nu_log, nu_log]))
        gamma = jnp.exp(nu_log + gamma_log) - 1.0
        lam = jnp.exp(-nu)
        a = jnp.broadcast_to(lam, u.shape)

        def combine(c1, c2):
            a1, x1 = c1
            a2, x2 = c2
            return (a1 * a2, x1 * a2 + x2)
        _, y = jax.lax.associative_scan(combine, (a, u), axis=1)
        u1, u2 = jnp.split(y, 2, axis=-1)
        x = (u1 + gamma * kv) / (u2 + gamma * k + 1e-06) * r
        return jnp.einsum('blu,uh->blh', x, W_o) + b_o

    def _L0_ffn_ref(x, W_r, W_k, W_v, mu_r, mu_k):
        import jax, jax.numpy as jnp
        import numpy as np
        DIM = 512

        def _reference_tuple_inner(x, W_r, W_k, W_v, mu_r, mu_k):
            B, T, C = x.shape
            x_prev = jnp.concatenate([jnp.zeros((B, 1, C), x.dtype), x[:, :-1, :]], axis=1)
            xr = mu_r * x + (1.0 - mu_r) * x_prev
            xk = mu_k * x + (1.0 - mu_k) * x_prev
            r = jax.nn.sigmoid(jnp.einsum('btc,dc->btd', xr, W_r))
            k = jnp.einsum('btc,dc->btd', xk, W_k)
            k_act = jnp.square(jax.nn.relu(k))
            out = r * jnp.einsum('btc,dc->btd', k_act, W_v)
            new_state = x[:, -1, :]
            return (out, new_state)
        return _reference_tuple_inner(x, W_r, W_k, W_v, mu_r, mu_k)[0]
    x = L0_attn_inputs
    x = _layernorm(x + _L0_attn_ref(x, L0_attn_W_rkv, L0_attn_b_rkv, L0_attn_W_o, L0_attn_b_o, L0_attn_nu_log, L0_attn_gamma_log), axis=-1)
    x = _layernorm(x + _L0_ffn_ref(x, L0_ffn_W_r, L0_ffn_W_k, L0_ffn_W_v, L0_ffn_mu_r, L0_ffn_mu_k), axis=-1)
    return x

_drawn_inputs = setup_inputs


def setup_inputs(seed=0):
    import zlib

    import numpy as np

    out = dict(_drawn_inputs(seed))
    spreads = {'L0_attn_b_rkv': (0.0, 0.1), 'L0_attn_b_o': (0.0, 0.1), 'L0_attn_gamma_log': (0.0, 2.0)}
    factors = {'L0_ffn_W_r': 3.044, 'L0_ffn_mu_r': 6.332}
    for name, (base, spread) in spreads.items():
        noise = np.random.default_rng([zlib.crc32(name.encode()), seed]).standard_normal(out[name].shape)
        drawn = base * np.exp(spread * noise) if base else spread * noise
        out[name] = jnp.asarray(drawn.astype(out[name].dtype))
    for name, factor in factors.items():
        out[name] = (out[name] * factor).astype(out[name].dtype)
    return out
```

```python
import math
from contextlib import ExitStack

import concourse.bass as bass
from concourse import mybir

F32 = mybir.dt.float32
F32R = mybir.dt.float32r
ALU = mybir.AluOpType
ACT = mybir.ActivationFunctionType

P = 128
H = 512
NC = H // P
TB = 512
NT = TB // P
HALF = TB // 2
HT = NT // 2
NH = 2
EPS_LN = 1e-5
EPS_DEN = 1e-6


class Step:

    def __init__(self, per_batch, s=None, batch=None, j=0, blocks=0):
        self.per_batch, self.batch, self.blocks = per_batch, batch, blocks
        self.s = s if batch is None else j

    def back(self, n):
        return Step(self.per_batch, self.s - n if self.batch is None else None, self.batch, self.s - n, self.blocks)

    def exists(self):
        return self.batch is not None or 0 <= self.s < self.blocks

    def first_of_batch(self):
        return self.s % self.per_batch == 0

    def odd(self):
        return self.s % 2

    def block(self):
        return self.s if self.batch is None else self.batch * self.per_batch + self.s

    def count(self, per_step, n):
        if self.batch is None:
            v = per_step * self.s + n
            return v if v > 0 else None
        return self.batch * (per_step * self.per_batch) + (per_step * self.s + n)


def wait(eng, sem, value):
    if value is not None:
        eng.wait_ge(sem, value)


OTHERS = [("V", 2, 2, 2), ("WO", 1, 0, 4), ("T", 1, 0, 2), ("T", 1, 2, 2), ("R", 1, 0, 2),
          ("K", 1, 0, 2), ("V", 1, 0, 2), ("R", 1, 2, 2), ("K", 1, 2, 2)]
SLOTS = [(name, back, first + i) for name, back, first, n in OTHERS for i in range(n)]
NBANK = 4


def slot_of(name, index):
    return [n for n, (what, _, i) in enumerate(SLOTS) if what == name and i == index][0]


def program(nc, xT, x, w_rkv, w_o, w_r, w_k, w_v, b_rkv, b_o, nu_log, gamma_log, mu_r, mu_k, out, seq):
    tokens = x.shape[0]
    blocks = tokens // TB
    per_batch = seq // TB
    batches = blocks // per_batch
    assert len(SLOTS) % NBANK == 0 and (3 * NC) % NBANK == 0 and per_batch % 2 == 0

    x_rows = x.rearrange("(n p) h -> n p h", p=P)
    out_rows = out.rearrange("(n p) h -> n p h", p=P)

    with ExitStack() as ctx:
        def sb(name, shape, dt=F32):
            return ctx.enter_context(nc.sbuf_tensor(name, shape, dt))

        def sem(name):
            return ctx.enter_context(nc.semaphore(name))

        def split(name, shape):
            hi = sb(name + "_hi", shape, F32R)
            value = sb(name + "_f", shape, F32)
            size = 4 * math.prod(shape[1:])
            lo = nc.alloc_sbuf_tensor_at(name + "_lo", shape, F32R, offset=nc.sbuf_base - size)
            return hi, lo, value

        wrkv_hi, wrkv_lo, wrkv_f = split("wrkv", [P, NC, 3, NC, P])
        wo_hi, wo_lo, wo_f = split("wo", [P, NC, H])
        wr_hi, wr_lo, wr_f = split("wr", [P, NC, H])
        wk_hi, wk_lo, wk_f = split("wk", [P, NC, H])
        wv_hi, wv_lo, wv_f = split("wv", [P, NC, H])
        x_hi, x_lo, x_f = split("x", [P, NC, TB])
        att_hi, att_lo, att_f = split("att", [P, NC, TB])
        xk_hi, xk_lo, xk_f = split("xk", [P, NC, HALF])
        xr_hi, xr_lo, xr_f = split("xr", [P, NC, HALF])
        ka_hi, ka_lo, ka_f = split("ka", [P, NC, HALF])

        y = sb("y", [P, 6, H])
        t = sb("t", [P, NT, H])
        gate = sb("gate", [P, 2, TB])
        key = sb("key", [P, 2, TB])
        kv = sb("kv", [P, TB])
        u2 = sb("u2", [P, TB])
        zT = sb("zT", [P, NC, HALF + 1])
        bo = sb("bo", [P, H])
        ident = sb("ident", [P, P])
        carry = sb("carry", [P, 2, NC])
        b_sb = sb("b_sb", [P, 3, NC])
        vecs = sb("vecs", [P, 4, NC])
        neg_br = sb("neg_br", [P, NC])
        nu = sb("nu", [P, NC])
        lam = sb("lam", [P, NC])
        ngsum = sb("ngsum", [P, NC])
        gamma = sb("gamma", [P, NC])
        om_mu = sb("om_mu", [P, 2, NC])
        half_pow = sb("half_pow", [P, HT])
        st = sb("st", [P, 2, NT, 6])
        held = sb("held", [P, 1])
        mv = sb("mv", [P, 2, NT, 2])
        ve = sb("ve", [P, 2, NT])
        rstd = sb("rstd", [P, 2, NT])

        bankA = [ctx.enter_context(nc.psum_tensor(f"bankA{i}", [P, TB], F32)) for i in range(NBANK)]
        bankB = [ctx.enter_context(nc.psum_tensor(f"bankB{i}", [P, 512], F32)) for i in range(NBANK)]

        def psum_of(name, index):
            return bankB[slot_of(name, index) % NBANK]

        def y_slot(s, tile):
            return tile if tile < HT else tile + HT * s.odd()

        s_wload = [sem(f"weights_loaded{i}") for i in range(8)]
        s_whi = sem("weights_hi")
        s_wlo = sem("weights_lo")
        s_small = sem("vectors_loaded")
        s_const = sem("constants_made")
        s_actc = sem("act_constants")
        s_dvec = sem("dve_constants")
        s_id = sem("identity_made")
        s_col0 = sem("previous_column")
        k_ready, v_ready, r_ready = sem("k_ready"), sem("v_ready"), sem("r_ready")
        ready = {n: sem(n + "_ready") for n in ("WO", "T", "R", "K", "V")}
        x_loaded = [sem(f"x_loaded{c}") for c in range(NC)]
        y_loaded = [sem(f"y_loaded{i}") for i in range(NT)]
        stored = [sem(f"stored{i}") for i in range(NT)]
        x_hi_made, x_lo_made = sem("x_hi_made"), sem("x_lo_made")
        att_hi_made, att_lo_made = sem("att_hi_made"), sem("att_lo_made")
        xk_hi_made, xk_lo_made = sem("xk_hi_made"), sem("xk_lo_made")
        xr_hi_made, xr_lo_made = sem("xr_hi_made"), sem("xr_lo_made")
        ka_hi_made, ka_lo_made = sem("ka_hi_made"), sem("ka_lo_made")
        key_exp, gate_exp, gate_plus1 = sem("key_exp"), sem("gate_exp"), sem("gate_plus1")
        kv_made, u2_scanned, u2_saved, den_made = sem("kv_made"), sem("u2_scanned"), sem("u2_saved"), sem("den_made")
        scale_made, rec_made = sem("scale_made"), sem("rec_made")
        u1_scanned, u1_saved, num_made, att_made = sem("u1_scanned"), sem("u1_saved"), sem("num_made"), sem("att_made")
        y_biased, y_made, z_made = sem("y_biased"), sem("y_made"), sem("z_made")
        ln_stats = [sem(f"ln{i}_stats") for i in (1, 2)]
        ln_mean = [sem(f"ln{i}_mean") for i in (1, 2)]
        ln_var = [sem(f"ln{i}_var") for i in (1, 2)]
        ln_rstd = [sem(f"ln{i}_rstd") for i in (1, 2)]
        zT_copied, xk_scaled, xr_scaled = sem("zT_copied"), sem("xk_scaled"), sem("xr_scaled")
        xk_made, xr_made = sem("xk_made"), sem("xr_made")
        tanh_made, relu_made, sq_made = sem("tanh_made"), sem("relu_made"), sem("sq_made")
        o_made, y2_made, out_made = sem("o_made"), sem("y2_made"), sem("out_made")

        taken = {"V": o_made, "WO": y_made, "T": zT_copied, "R": tanh_made, "K": relu_made}

        weights = [(wrkv_hi[:, c], wrkv_lo[:, c], wrkv_f[:, c], w_rkv[:, c], 1.0) for c in range(NC)]
        weights += [(wo_hi[:], wo_lo[:], wo_f[:], w_o, 1.0), (wr_hi[:], wr_lo[:], wr_f[:], w_r, 1.0),
                    (wk_hi[:], wk_lo[:], wk_f[:], w_k, 1.0), (wv_hi[:], wv_lo[:], wv_f[:], w_v, 0.5)]
        W_WO, W_R, W_K, W_V = NC, NC + 1, NC + 2, NC + 3

        def steps(eng, step):
            for s in range(per_batch - 1):
                step(Step(per_batch, s=s, blocks=blocks))
            with eng.Fori(1, batches) as batch:
                for j in range(-1, per_batch - 1):
                    step(Step(per_batch, batch=batch, j=j, blocks=blocks))
            for s in range(blocks - 1, blocks + 2):
                step(Step(per_batch, s=s, blocks=blocks))

        block = ctx.enter_context(nc.Block())

        @block.sync
        def _(sp):
            sp.dma_start(b_sb[:], b_rkv).then_inc(s_small, 16)
            for i, v in enumerate((nu_log, gamma_log, mu_r, mu_k)):
                sp.dma_start(vecs[:, i], v).then_inc(s_small, 16)
            sp.dma_start(bo[:], b_o).then_inc(s_small, 16)
            for c in range(NC):
                sp.dma_start(x_f[:, c], xT[0, :, c]).then_inc(x_loaded[c], 16)
                if c == 0:
                    sp.dma_start(weights[0][2], weights[0][3]).then_inc(s_wload[0], 16)
            for i in range(1, len(weights)):
                sp.dma_start(weights[i][2], weights[i][3]).then_inc(s_wload[i], 16)

            def store(s, half):
                for i in range(HT):
                    wait(sp, out_made, s.count(NT, HT * half + i + 1))
                    sp.dma_start(out_rows[s.block() * NT + (HT * half + i)], t[:, HT * half + i])\
                        .then_inc(stored[HT * half + i], 16)

            def load_rows(s, half, user):
                for i in range(HT):
                    tile = HT * half + i
                    wait(sp, y2_made, user.count(NT, tile + 1))
                    sp.dma_start(y[:, y_slot(s, tile)], x_rows[s.block() * NT + tile]).then_inc(y_loaded[tile], 16)

            def load_xT(s):
                wait(sp, r_ready, s.back(1).count(NC, NC))
                for c in range(NC):
                    sp.dma_start(x_f[:, c], xT[s.block(), :, c]).then_inc(x_loaded[c], 16)

            def step(s):
                if s.back(2).exists():
                    store(s.back(2), 1)
                if s.exists():
                    load_rows(s, 1, s.back(2))
                    if s.back(-1).exists():
                        load_xT(s.back(-1))
                    load_rows(s, 0, s.back(1))
                if s.back(1).exists():
                    store(s.back(1), 0)

            steps(sp, step)
            for tile in range(NT):
                sp.wait_ge(stored[tile], 16 * blocks)

        @block.gpsimd
        def _(pool):
            pool.memset(ident[:], 0.0).then_inc(s_id, 1)
            pool.memset(half_pow[:], -0.5).then_inc(s_const, 1)
            pool.wait_ge(s_id, 1)
            pool.affine_select(out=ident[:], in_=ident[:], compare_op=ALU.not_equal, fill=1.0,
                               base=0, pattern=[[-1, P]], channel_multiplier=1).then_inc(s_id, 1)
            pool.wait_ge(s_small, 96)

            def att(s, c):
                wait(pool, num_made, s.count(NC, c + 1))
                wait(pool, rec_made, s.count(NC, c + 1))
                pool.tensor_tensor(att_f[:, c], att_f[:, c], gate[:, c % 2], ALU.mult).then_inc(att_made, 1)

            def att_low(s, c):
                wait(pool, att_hi_made, s.count(NC, c + 1))
                pool.tensor_tensor(att_lo[:, c], att_f[:, c], att_hi[:, c], ALU.subtract).then_inc(att_lo_made, 1)

            def inverse_std(s, which, half):
                wait(pool, ln_var[which], s.count(NH, half + 1))
                tiles = slice(HT * half, HT * half + HT)
                pool.tensor_tensor(rstd[:, which, tiles], ve[:, which, tiles], half_pow[:], ALU.pow)\
                    .then_inc(ln_rstd[which], 1)

            def mixed_low(s, half):
                for lo, f, hi, hi_made, lo_made in ((xr_lo, xr_f, xr_hi, xr_hi_made, xr_lo_made),
                                                    (xk_lo, xk_f, xk_hi, xk_hi_made, xk_lo_made)):
                    wait(pool, hi_made, s.count(NH, half + 1))
                    pool.tensor_tensor(lo[:], f[:], hi[:], ALU.subtract).then_inc(lo_made, 1)

            def residual(s, half):
                for i in range(HT):
                    tile = HT * half + i
                    wait(pool, o_made, s.count(NT, tile + 1))
                    pool.tensor_tensor(t[:, tile], t[:, tile], y[:, y_slot(s, tile)], ALU.add).then_inc(y2_made, 1)

            def bias_rows(s):
                for tile in (2, 3, 0, 1):
                    wait(pool, y_loaded[tile], s.count(16, 16))
                    rows = y[:, y_slot(s, tile)]
                    pool.tensor_tensor(rows, rows, bo[:], ALU.add).then_inc(y_biased, 1)

            def step(s):
                s1, s2 = s.back(1), s.back(2)
                if s2.exists():
                    residual(s2, 1)
                if s1.exists():
                    inverse_std(s1, 0, 0)
                if s2.exists():
                    inverse_std(s2, 1, 1)
                if s1.exists():
                    inverse_std(s1, 0, 1)
                if s.exists():
                    att(s, 0)
                    att_low(s, 0)
                if s1.exists():
                    mixed_low(s1, 0)
                if s.exists():
                    att(s, 1)
                    att_low(s, 1)
                    att(s, 2)
                    att_low(s, 2)
                if s1.exists():
                    mixed_low(s1, 1)
                    residual(s1, 0)
                if s.exists():
                    att(s, 3)
                    att_low(s, 3)
                if s1.exists():
                    inverse_std(s1, 1, 0)
                if s.exists():
                    bias_rows(s)

            steps(pool, step)

        @block.scalar
        def _(act):
            def x_high(s):
                for c in range(NC):
                    wait(act, x_loaded[c], s.count(16, 16))
                    wait(act, r_ready, s.back(1).count(NC, NC))
                    act.activation(x_hi[:, c], x_f[:, c], ACT.Copy).then_inc(x_hi_made, 1)

            def weight_high(i):
                hi, _, f, _, factor = weights[i]
                act.wait_ge(s_wload[i], 16)
                act.activation(hi, f, ACT.Copy, scale=factor).then_inc(s_whi, 1)

            def exp_key(s, c):
                wait(act, k_ready, s.count(NC, c + 1))
                wait(act, scale_made, s.count(NC, c - 1))
                act.activation(key[:, c % 2], bankA[(3 * c) % NBANK][:], ACT.Exp, bias=b_sb[:, 0, c:c + 1])\
                    .then_inc(key_exp, 1)

            def exp_gate(s, c):
                wait(act, r_ready, s.count(NC, c + 1))
                wait(act, att_made, s.count(NC, c - 1))
                act.activation(gate[:, c % 2], bankA[(3 * c + 2) % NBANK][:], ACT.Exp, bias=neg_br[:, c:c + 1],
                               scale=-1.0).then_inc(gate_exp, 1)
                wait(act, gate_exp, s.count(NC, c + 1))
                act.activation(gate[:, c % 2], gate[:, c % 2], ACT.Copy, bias=1.0).then_inc(gate_plus1, 1)

            def att_high(s, c):
                wait(act, att_made, s.count(NC, c + 1))
                act.activation(att_hi[:, c], att_f[:, c], ACT.Copy).then_inc(att_hi_made, 1)

            def copy_zT(s, half):
                wait(act, s_col0, s.count(NH, half + 1))
                for i in range(2):
                    wait(act, ready["T"], s.count(NT, 2 * half + i + 1))
                    src = psum_of("T", 2 * half + i)[:].rearrange("p (c n) -> p c n", c=2)
                    act.activation(zT[:, 2 * i:2 * i + 2, 1:HALF + 1], src, ACT.Copy).then_inc(zT_copied, 1)

            def previous_scaled(s, half):
                wait(act, zT_copied, s.count(NT, 2 * half + 2))
                for f, which, made, through in ((xr_f, 0, xr_scaled, "R"), (xk_f, 1, xk_scaled, "K")):
                    wait(act, ready[through], s.count(NT, 2 * half))
                    for c in range(NC):
                        act.activation(f[:, c], zT[:, c, 0:HALF], ACT.Copy, scale=om_mu[:, which, c:c + 1])\
                            .then_inc(made, 1)

            def mixed_high(s, half):
                for hi, f, made, hi_made in ((xr_hi, xr_f, xr_made, xr_hi_made), (xk_hi, xk_f, xk_made, xk_hi_made)):
                    wait(act, made, s.count(NH * NC, NC * half + NC))
                    act.activation(hi[:], f[:], ACT.Copy).then_inc(hi_made, 1)

            def tanh(s, half):
                for i in range(HT):
                    tile = HT * half + i
                    wait(act, ready["R"], s.count(NT, tile + 1))
                    wait(act, stored[tile], s.back(1).count(16, 16))
                    act.activation(t[:, tile], psum_of("R", tile)[:], ACT.Tanh, scale=0.5).then_inc(tanh_made, 1)

            def key_square(s, half):
                for i in range(2):
                    n = 2 * half + i
                    part = slice(2 * i, 2 * i + 2)
                    src = psum_of("K", n)[:].rearrange("p (c n) -> p c n", c=2)
                    wait(act, ready["K"], s.count(NT, n + 1))
                    wait(act, ready["V"], s.count(NT, 2 * half))
                    act.activation(ka_f[:, part], src, ACT.Relu).then_inc(relu_made, 1)
                    wait(act, relu_made, s.count(NT, n + 1))
                    act.activation(ka_hi[:, part], ka_f[:, part], ACT.Square).then_inc(ka_hi_made, 1)
                    wait(act, ka_hi_made, s.count(NT, n + 1))
                    act.activation(ka_f[:, part], ka_f[:, part], ACT.Square).then_inc(sq_made, 1)

            act.wait_ge(s_small, 96)
            act.activation(nu[:], vecs[:, 0], ACT.Exp).then_inc(s_actc, 1)
            act.wait_ge(s_actc, 1)
            act.activation(lam[:], nu[:], ACT.Exp, scale=-1.0).then_inc(s_actc, 1)
            act.wait_ge(s_dvec, 1)
            act.activation(gamma[:], ngsum[:], ACT.Exp).then_inc(s_actc, 1)
            act.wait_ge(s_dvec, 4)
            x_high(Step(per_batch, s=0, blocks=blocks))
            for i in range(len(weights)):
                weight_high(i)

            def step(s):
                s1 = s.back(1)
                if s.exists():
                    exp_key(s, 0)
                    exp_gate(s, 0)
                    exp_key(s, 1)
                if s1.exists():
                    copy_zT(s1, 0)
                    previous_scaled(s1, 0)
                if s.exists():
                    att_high(s, 0)
                    exp_gate(s, 1)
                if s1.exists():
                    mixed_high(s1, 0)
                if s.exists():
                    exp_key(s, 2)
                    exp_gate(s, 2)
                    att_high(s, 1)
                if s1.exists():
                    copy_zT(s1, 1)
                    tanh(s1, 0)
                    key_square(s1, 0)
                    previous_scaled(s1, 1)
                if s.exists():
                    att_high(s, 2)
                    exp_key(s, 3)
                    exp_gate(s, 3)
                if s1.exists():
                    mixed_high(s1, 1)
                if s.exists():
                    if s.back(-1).exists():
                        x_high(s.back(-1))
                    att_high(s, 3)
                if s1.exists():
                    tanh(s1, 1)
                    key_square(s1, 1)

            steps(act, step)

        @block.vector
        def _(dve):
            dve.memset(zT[:, :, 0:1], 0.0).then_inc(s_col0, 1)
            dve.wait_ge(s_small, 96)
            dve.tensor_tensor(ngsum[:], vecs[:, 0], vecs[:, 1], ALU.add).then_inc(s_dvec, 1)
            dve.tensor_scalar(neg_br[:], b_sb[:, 2], -1.0, None, ALU.mult).then_inc(s_dvec, 1)
            dve.tensor_scalar(om_mu[:], vecs[:, 2:4], -1.0, 1.0, ALU.mult, ALU.add).then_inc(s_dvec, 1)
            dve.wait_ge(s_actc, 3)
            dve.tensor_scalar(gamma[:], gamma[:], -1.0, None, ALU.add).then_inc(s_dvec, 1)
            for c in range(NC):
                dve.wait_ge(x_hi_made, c + 1)
                dve.tensor_tensor(x_lo[:, c], x_f[:, c], x_hi[:, c], ALU.subtract).then_inc(x_lo_made, 1)
            for i, (hi, lo, f, _, factor) in enumerate(weights):
                dve.wait_ge(s_whi, i + 1)
                dve.scalar_tensor_tensor(out=lo, in0=f, scalar=factor, in1=hi, op0=ALU.mult, op1=ALU.subtract)\
                    .then_inc(s_wlo, 1)
            dve.wait_ge(s_dvec, 4)

            def x_low(s):
                for c in range(NC):
                    wait(dve, x_hi_made, s.count(NC, c + 1))
                    dve.tensor_tensor(x_lo[:, c], x_f[:, c], x_hi[:, c], ALU.subtract).then_inc(x_lo_made, 1)

            def state(s, which, c):
                return 0.0 if s.first_of_batch() else carry[:, which, c:c + 1]

            def denominator(s, c):
                lam_c = lam[:, c:c + 1].to_broadcast([P, TB])
                wait(dve, key_exp, s.count(NC, c + 1))
                wait(dve, u2_saved, s.count(NC, c))
                wait(dve, den_made, s.count(NC, c))
                dve.tensor_tensor_scan(u2[:], lam_c, key[:, c % 2], state(s, 1, c), ALU.mult, ALU.add)\
                    .then_inc(u2_scanned, 1)
                wait(dve, v_ready, s.count(NC, c + 1))
                wait(dve, num_made, s.count(NC, c))
                dve.scalar_tensor_tensor(out=kv[:], in0=bankA[(3 * c + 1) % NBANK][:], scalar=b_sb[:, 1, c:c + 1],
                                         in1=key[:, c % 2], op0=ALU.add, op1=ALU.mult).then_inc(kv_made, 1)
                wait(dve, u2_scanned, s.count(NC, c + 1))
                dve.tensor_copy(carry[:, 1, c:c + 1], u2[:, TB - 1:TB]).then_inc(u2_saved, 1)
                wait(dve, kv_made, s.count(NC, c + 1))
                dve.scalar_tensor_tensor(out=key[:, c % 2], in0=key[:, c % 2], scalar=gamma[:, c:c + 1], in1=u2[:],
                                         op0=ALU.mult, op1=ALU.add).then_inc(den_made, 1)
                wait(dve, den_made, s.count(NC, c + 1))
                wait(dve, gate_plus1, s.count(NC, c + 1))
                dve.scalar_tensor_tensor(out=gate[:, c % 2], in0=key[:, c % 2], scalar=EPS_DEN, in1=gate[:, c % 2],
                                         op0=ALU.add, op1=ALU.mult).then_inc(scale_made, 1)
                wait(dve, scale_made, s.count(NC, c + 1))
                dve.reciprocal(gate[:, c % 2], gate[:, c % 2]).then_inc(rec_made, 1)

            def numerator(s, c):
                lam_c = lam[:, c:c + 1].to_broadcast([P, TB])
                wait(dve, ready["WO"], s.back(1).count(NT, NT))
                wait(dve, kv_made, s.count(NC, c + 1))
                wait(dve, u1_saved, s.count(NC, c))
                dve.tensor_tensor_scan(att_f[:, c], lam_c, kv[:], state(s, 0, c), ALU.mult, ALU.add)\
                    .then_inc(u1_scanned, 1)
                wait(dve, u1_scanned, s.count(NC, c + 1))
                dve.tensor_copy(carry[:, 0, c:c + 1], att_f[:, c, TB - 1:TB]).then_inc(u1_saved, 1)
                wait(dve, u1_saved, s.count(NC, c + 1))
                dve.scalar_tensor_tensor(out=att_f[:, c], in0=kv[:], scalar=gamma[:, c:c + 1], in1=att_f[:, c],
                                         op0=ALU.mult, op1=ALU.add).then_inc(num_made, 1)

            def statistics(s, which, half, rows, made):
                for i in range(HT):
                    tile = HT * half + i
                    wait(dve, made, s.count(NT, tile + 1))
                    dve.bn_stats(st[:, which, tile], rows(tile)).then_inc(ln_stats[which], 1)
                wait(dve, ln_stats[which], s.count(NT, HT * half + HT))
                dve.memset(held[:], 0.0)
                for i in range(HT):
                    tile = HT * half + i
                    dve.bn_aggr(mv[:, which, tile], st[:, which, tile]).then_inc(ln_mean[which], 1)
                wait(dve, ln_mean[which], s.count(NT, HT * half + HT))
                tiles = slice(HT * half, HT * half + HT)
                dve.tensor_scalar(ve[:, which, tiles], mv[:, which, tiles, 1], EPS_LN, None, ALU.add)\
                    .then_inc(ln_var[which], 1)

            def attention_rows(s, half):
                for i in range(HT):
                    tile = HT * half + i
                    rows = y[:, y_slot(s, tile)]
                    wait(dve, ready["WO"], s.count(NT, tile + 1))
                    wait(dve, y_biased, s.count(NT, NT))
                    dve.tensor_tensor(rows, psum_of("WO", tile)[:], rows, ALU.add).then_inc(y_made, 1)
                statistics(s, 0, half, lambda tile: y[:, y_slot(s, tile)], y_made)

            def normalise(s, which, half, rows, done):
                wait(dve, ln_rstd[which], s.count(NH, half + 1))
                for i in range(HT):
                    tile = HT * half + i
                    dve.tensor_scalar(rows(tile), rows(tile), mv[:, which, tile, 0:1], rstd[:, which, tile:tile + 1],
                                      ALU.subtract, ALU.mult).then_inc(done, 1)

            def mix(s, half, next_starts_batch):
                for f, which, scaled, made in ((xr_f, 0, xr_scaled, xr_made), (xk_f, 1, xk_scaled, xk_made)):
                    for c in range(NC):
                        wait(dve, scaled, s.count(NH * NC, NC * half + c + 1))
                        dve.scalar_tensor_tensor(out=f[:, c], in0=zT[:, c, 1:HALF + 1],
                                                 scalar=vecs[:, 2 + which, c:c + 1], in1=f[:, c],
                                                 op0=ALU.mult, op1=ALU.add).then_inc(made, 1)
                if next_starts_batch:
                    dve.memset(zT[:, :, 0:1], 0.0).then_inc(s_col0, 1)
                else:
                    dve.tensor_copy(zT[:, :, 0:1], zT[:, :, HALF:HALF + 1]).then_inc(s_col0, 1)

            def key_low(s, half):
                for i in range(2):
                    part = slice(2 * i, 2 * i + 2)
                    wait(dve, sq_made, s.count(NT, 2 * half + i + 1))
                    dve.tensor_tensor(ka_lo[:, part], ka_f[:, part], ka_hi[:, part], ALU.subtract)\
                        .then_inc(ka_lo_made, 1)

            def gated_values(s, half):
                for i in range(HT):
                    tile = HT * half + i
                    wait(dve, ready["V"], s.count(NT, tile + 1))
                    wait(dve, tanh_made, s.count(NT, tile + 1))
                    dve.scalar_tensor_tensor(out=t[:, tile], in0=t[:, tile], scalar=1.0, in1=psum_of("V", tile)[:],
                                             op0=ALU.add, op1=ALU.mult).then_inc(o_made, 1)

            def result_rows(s):
                return lambda tile: t[:, tile]

            def z_rows(s):
                return lambda tile: y[:, y_slot(s, tile)]

            def step(s):
                s1, s2 = s.back(1), s.back(2)
                if s.exists():
                    denominator(s, 0)
                if s2.exists():
                    gated_values(s2, 1)
                if s1.exists():
                    attention_rows(s1, 0)
                if s2.exists():
                    statistics(s2, 1, 1, result_rows(s2), y2_made)
                if s1.exists():
                    normalise(s1, 0, 0, z_rows(s1), z_made)
                    attention_rows(s1, 1)
                if s2.exists():
                    normalise(s2, 1, 1, result_rows(s2), out_made)
                if s1.exists():
                    normalise(s1, 0, 1, z_rows(s1), z_made)
                if s.exists():
                    numerator(s, 0)
                if s1.exists():
                    mix(s1, 0, False)
                if s.exists():
                    denominator(s, 1)
                    numerator(s, 1)
                    denominator(s, 2)
                    numerator(s, 2)
                if s1.exists():
                    key_low(s1, 0)
                    mix(s1, 1, s.first_of_batch())
                if s.exists():
                    denominator(s, 3)
                if s1.exists():
                    gated_values(s1, 0)
                if s.exists():
                    if s.back(-1).exists():
                        x_low(s.back(-1))
                    numerator(s, 3)
                if s1.exists():
                    statistics(s1, 1, 0, result_rows(s1), y2_made)
                    normalise(s1, 1, 0, result_rows(s1), out_made)
                    key_low(s1, 1)

            steps(dve, step)

        @block.tensor
        def _(pe):
            def project(s, c, which):
                n = 3 * c + which
                m = n - NBANK
                of = s if m >= 0 else s.back(1)
                m %= 3 * NC
                wait(pe, (key_exp, kv_made, gate_exp)[m % 3], of.count(NC, m // 3 + 1))
                bank = bankA[n % NBANK]
                if s.batch is None and s.s == 0:
                    pe.wait_ge(s_wlo, c + 1)
                for h in range(NC):
                    if n == 0:
                        wait(pe, x_lo_made, s.count(NC, h + 1))
                    w_hi, w_lo = wrkv_hi[:, c, which, h], wrkv_lo[:, c, which, h]
                    pe.matmul(bank[:], w_hi, x_hi[:, h], start=(h == 0), stop=False)
                    pe.matmul(bank[:], w_hi, x_lo[:, h], start=False, stop=False)
                    last = pe.matmul(bank[:], w_lo, x_hi[:, h], start=False, stop=(h == NC - 1))
                last.then_inc((k_ready, v_ready, r_ready)[which], 1)

            def bank_free(s, name, index):
                n = slot_of(name, index) - NBANK
                at = s if n >= 0 else s.back(1)
                what, back, i = SLOTS[n % len(SLOTS)]
                wait(pe, taken[what], at.back(back).count(NT, i + 1))

            def rows_product(s, name, index, a_hi, a_lo, tokens_at, w_hi, w_lo):
                bank = psum_of(name, index)
                for c in range(NC):
                    hi, lo = a_hi[:, c, tokens_at:tokens_at + P], a_lo[:, c, tokens_at:tokens_at + P]
                    pe.matmul(bank[:], hi, w_hi[:, c], start=(c == 0), stop=False)
                    pe.matmul(bank[:], hi, w_lo[:, c], start=False, stop=False)
                    last = pe.matmul(bank[:], lo, w_hi[:, c], start=False, stop=(c == NC - 1))
                last.then_inc(ready[name], 1)

            def attention_out(s, run):
                for tile in range(NT):
                    bank_free(run, "WO", tile)
                    if tile == 0:
                        wait(pe, att_lo_made, s.count(NC, NC))
                    if s.batch is None and s.s == 0:
                        pe.wait_ge(s_wlo, W_WO + 1)
                    rows_product(s, "WO", tile, att_hi, att_lo, tile * P, wo_hi, wo_lo)

            def transposes(s, half, run):
                for i in range(2):
                    n = 2 * half + i
                    bank_free(run, "T", n)
                    wait(pe, z_made, s.count(NT, HT * half + HT))
                    if s.batch is None and s.s == 0:
                        pe.wait_ge(s_id, 2)
                    for c in range(2):
                        for tile in range(HT):
                            at = c * HALF + tile * P
                            chunk = 2 * i + c
                            rows = y[:, y_slot(s, HT * half + tile), chunk * P:(chunk + 1) * P]
                            last = pe.transpose(psum_of("T", n)[:, at:at + P], rows, ident[:])
                    last.then_inc(ready["T"], 1)

            def receptance(s, half, run):
                for i in range(HT):
                    bank_free(run, "R", HT * half + i)
                    wait(pe, xr_lo_made, s.count(NH, half + 1))
                    if s.batch is None and s.s == 0:
                        pe.wait_ge(s_wlo, W_R + 1)
                    rows_product(s, "R", HT * half + i, xr_hi, xr_lo, i * P, wr_hi, wr_lo)

            def keys(s, half, run):
                for i in range(2):
                    n = 2 * half + i
                    bank_free(run, "K", n)
                    wait(pe, xk_lo_made, s.count(NH, half + 1))
                    if s.batch is None and s.s == 0:
                        pe.wait_ge(s_wlo, W_K + 1)
                    for d in range(2):
                        dst = psum_of("K", n)[:, d * HALF:(d + 1) * HALF]
                        cols = slice((2 * i + d) * P, (2 * i + d + 1) * P)
                        for c in range(NC):
                            pe.matmul(dst, wk_hi[:, c, cols], xk_hi[:, c], start=(c == 0), stop=False)
                            pe.matmul(dst, wk_hi[:, c, cols], xk_lo[:, c], start=False, stop=False)
                            last = pe.matmul(dst, wk_lo[:, c, cols], xk_hi[:, c], start=False, stop=(c == NC - 1))
                    last.then_inc(ready["K"], 1)

            def values(s, half, run):
                for i in range(HT):
                    bank_free(run, "V", HT * half + i)
                    wait(pe, ka_lo_made, s.count(NT, 2 * half + 2))
                    if s.batch is None and s.s == 0:
                        pe.wait_ge(s_wlo, W_V + 1)
                    rows_product(s, "V", HT * half + i, ka_hi, ka_lo, i * P, wv_hi, wv_lo)

            def step(s):
                s1, s2 = s.back(1), s.back(2)
                if s.exists():
                    for which in range(3):
                        project(s, 0, which)
                if s2.exists():
                    values(s2, 1, s)
                if s1.exists():
                    attention_out(s1, s)
                if s.exists():
                    project(s, 1, 0)
                if s1.exists():
                    transposes(s1, 0, s)
                if s.exists():
                    project(s, 1, 1)
                    project(s, 1, 2)
                    for which in range(3):
                        project(s, 2, which)
                if s1.exists():
                    transposes(s1, 1, s)
                    receptance(s1, 0, s)
                    keys(s1, 0, s)
                if s.exists():
                    for which in range(3):
                        project(s, 3, which)
                if s1.exists():
                    values(s1, 0, s)
                    receptance(s1, 1, s)
                    keys(s1, 1, s)

            steps(pe, step)


def kernel(**inputs):
    import numpy as np
    import concourse.bacc as bacc
    from concourse.bass_utils import run_bass_kernel_spmd

    x = np.asarray(inputs["L0_attn_inputs"])
    B, L, Hx = x.shape
    tokens = B * L
    rows = x.reshape(tokens, Hx)
    xT = rows.reshape(tokens // TB, TB, NC, P).transpose(0, 3, 2, 1)
    w = np.asarray(inputs["L0_attn_W_rkv"]).reshape(NC, P, 3, NC, P)[:, :, [1, 2, 0]].transpose(1, 3, 2, 0, 4)

    def by_input(m):
        return np.asarray(m).reshape(NC, P, H).transpose(1, 0, 2)

    def by_channel(v):
        return np.asarray(v).reshape(NC, P).T

    arrays = {
        "xT": xT, "x": rows, "w_rkv": w,
        "w_o": by_input(inputs["L0_attn_W_o"]),
        "w_r": by_input(np.asarray(inputs["L0_ffn_W_r"]).T),
        "w_k": by_input(np.asarray(inputs["L0_ffn_W_k"]).T),
        "w_v": by_input(np.asarray(inputs["L0_ffn_W_v"]).T),
        "b_rkv": np.asarray(inputs["L0_attn_b_rkv"]).reshape(3, NC, P)[[1, 2, 0]].transpose(2, 0, 1),
        "b_o": np.broadcast_to(np.asarray(inputs["L0_attn_b_o"]), (P, H)),
        "nu_log": by_channel(inputs["L0_attn_nu_log"]),
        "gamma_log": by_channel(inputs["L0_attn_gamma_log"]),
        "mu_r": by_channel(inputs["L0_ffn_mu_r"]),
        "mu_k": by_channel(inputs["L0_ffn_mu_k"]),
    }
    nc = bacc.Bacc("TRN2", target_bir_lowering=False, num_devices=1)
    sent, aps = {}, []
    for name, a in arrays.items():
        a = np.ascontiguousarray(a)
        sent[f"in_{name}"] = a
        aps.append(nc.dram_tensor(f"in_{name}", a.shape, mybir.dt.from_np(a.dtype), kind="ExternalInput").ap())
    out = nc.dram_tensor("out", (tokens, Hx), F32, kind="ExternalOutput").ap()
    program(nc, *aps, out, L)
    r = run_bass_kernel_spmd(nc, [sent], core_ids=[0])
    return r.results[0]["out"].reshape(B, L, Hx)
```

```python
import math
from contextlib import ExitStack

import concourse.bass as bass
from concourse import mybir

F32 = mybir.dt.float32
F32R = mybir.dt.float32r
ALU = mybir.AluOpType
ACT = mybir.ActivationFunctionType

P = 128
H = 512
NC = H // P
TB = 512
NT = TB // P
HALF = TB // 2
HT = NT // 2
NH = 2
EPS_LN = 1e-5
EPS_DEN = 1e-6


class Step:

    def __init__(self, per_batch, s=None, batch=None, j=0, blocks=0):
        self.per_batch, self.batch, self.blocks = per_batch, batch, blocks
        self.s = s if batch is None else j

    def back(self, n):
        return Step(self.per_batch, self.s - n if self.batch is None else None, self.batch, self.s - n, self.blocks)

    def exists(self):
        return self.batch is not None or 0 <= self.s < self.blocks

    def first_of_batch(self):
        return self.s % self.per_batch == 0

    def odd(self):
        return self.s % 2

    def block(self):
        return self.s if self.batch is None else self.batch * self.per_batch + self.s

    def count(self, per_step, n):
        if self.batch is None:
            v = per_step * self.s + n
            return v if v > 0 else None
        return self.batch * (per_step * self.per_batch) + (per_step * self.s + n)


def wait(eng, sem, value):
    if value is not None:
        eng.wait_ge(sem, value)


OTHERS = [("V", 2, 2, 2), ("WO", 1, 0, 4), ("T", 1, 0, 2), ("T", 1, 2, 2), ("R", 1, 0, 2),
          ("K", 1, 0, 2), ("V", 1, 0, 2), ("R", 1, 2, 2), ("K", 1, 2, 2)]
SLOTS = [(name, back, first + i) for name, back, first, n in OTHERS for i in range(n)]
NBANK = 4


def slot_of(name, index):
    return [n for n, (what, _, i) in enumerate(SLOTS) if what == name and i == index][0]


def program(nc, xT, x, w_rkv, w_o, w_r, w_k, w_v, b_rkv, b_o, nu_log, gamma_log, mu_r, mu_k, out, seq):
    tokens = x.shape[0]
    blocks = tokens // TB
    per_batch = seq // TB
    batches = blocks // per_batch
    assert len(SLOTS) % NBANK == 0 and (3 * NC) % NBANK == 0 and per_batch % 2 == 0

    x_rows = x.rearrange("(n p) h -> n p h", p=P)
    out_rows = out.rearrange("(n p) h -> n p h", p=P)

    with ExitStack() as ctx:
        def sb(name, shape, dt=F32):
            return ctx.enter_context(nc.sbuf_tensor(name, shape, dt))

        def sem(name):
            return ctx.enter_context(nc.semaphore(name))

        def split(name, shape):
            hi = sb(name + "_hi", shape, F32R)
            value = sb(name + "_f", shape, F32)
            size = 4 * math.prod(shape[1:])
            lo = nc.alloc_sbuf_tensor_at(name + "_lo", shape, F32R, offset=nc.sbuf_base - size)
            return hi, lo, value

        wrkv_hi, wrkv_lo, wrkv_f = split("wrkv", [P, NC, 3, NC, P])
        wo_hi, wo_lo, wo_f = split("wo", [P, NC, H])
        wr_hi, wr_lo, wr_f = split("wr", [P, NC, H])
        wk_hi, wk_lo, wk_f = split("wk", [P, NC, H])
        wv_hi, wv_lo, wv_f = split("wv", [P, NC, H])
        x_hi, x_lo, x_f = split("x", [P, NC, TB])
        att_hi, att_lo, att_f = split("att", [P, NC, TB])
        xk_hi, xk_lo, xk_f = split("xk", [P, NC, HALF])
        xr_hi, xr_lo, xr_f = split("xr", [P, NC, HALF])
        ka_hi, ka_lo, ka_f = split("ka", [P, NC, HALF])

        y = sb("y", [P, 6, H])
        t = sb("t", [P, NT, H])
        gate = sb("gate", [P, 2, TB])
        key = sb("key", [P, 2, TB])
        kv = sb("kv", [P, TB])
        u2 = sb("u2", [P, TB])
        zT = sb("zT", [P, NC, HALF + 1])
        bo = sb("bo", [P, H])
        ident = sb("ident", [P, P])
        carry = sb("carry", [P, 2, NC])
        b_sb = sb("b_sb", [P, 3, NC])
        vecs = sb("vecs", [P, 4, NC])
        neg_br = sb("neg_br", [P, NC])
        nu = sb("nu", [P, NC])
        lam = sb("lam", [P, NC])
        ngsum = sb("ngsum", [P, NC])
        gamma = sb("gamma", [P, NC])
        om_mu = sb("om_mu", [P, 2, NC])
        half_pow = sb("half_pow", [P, HT])
        st = sb("st", [P, 2, NT, 6])
        held = sb("held", [P, 1])
        mv = sb("mv", [P, 2, NT, 2])
        ve = sb("ve", [P, 2, NT])
        rstd = sb("rstd", [P, 2, NT])

        bankA = [ctx.enter_context(nc.psum_tensor(f"bankA{i}", [P, TB], F32)) for i in range(NBANK)]
        bankB = [ctx.enter_context(nc.psum_tensor(f"bankB{i}", [P, 512], F32)) for i in range(NBANK)]

        def psum_of(name, index):
            return bankB[slot_of(name, index) % NBANK]

        def y_slot(s, tile):
            return tile if tile < HT else tile + HT * s.odd()

        wA_loaded = [sem(f"wA_loaded{i}") for i in range(6)]
        wA_hi_made, wA_lo_made = sem("wA_hi_made"), sem("wA_lo_made")
        w_loaded = [sem(f"w_loaded{i}") for i in range(4)]
        w_hi_made, w_lo_made, wv_halved = sem("w_hi_made"), sem("w_lo_made"), sem("wv_halved")
        s_small, s_bo = sem("vectors_loaded"), sem("bo_loaded")
        s_const = sem("constants_made")
        s_actc = sem("act_constants")
        s_dvec = sem("dve_constants")
        s_id = sem("identity_made")
        s_col0 = sem("previous_column")
        k_ready, v_ready, r_ready = sem("k_ready"), sem("v_ready"), sem("r_ready")
        ready = {n: sem(n + "_ready") for n in ("WO", "T", "R", "K", "V")}
        x_loaded = [sem(f"x_loaded{c}") for c in range(NC)]
        y_loaded = [sem(f"y_loaded{i}") for i in range(NT)]
        stored = [sem(f"stored{i}") for i in range(NT)]
        x_hi_made, x_lo_made = sem("x_hi_made"), sem("x_lo_made")
        att_hi_made, att_lo_made = sem("att_hi_made"), sem("att_lo_made")
        xk_hi_made, xk_lo_made = sem("xk_hi_made"), sem("xk_lo_made")
        xr_hi_made, xr_lo_made = sem("xr_hi_made"), sem("xr_lo_made")
        ka_hi_made, ka_lo_made = sem("ka_hi_made"), sem("ka_lo_made")
        key_exp, gate_exp, gate_plus1 = sem("key_exp"), sem("gate_exp"), sem("gate_plus1")
        kv_made, u2_scanned, u2_saved, den_made = sem("kv_made"), sem("u2_scanned"), sem("u2_saved"), sem("den_made")
        scale_made, rec_made = sem("scale_made"), sem("rec_made")
        u1_scanned, u1_saved, num_made, att_made = sem("u1_scanned"), sem("u1_saved"), sem("num_made"), sem("att_made")
        y_biased, y_made, z_made = sem("y_biased"), sem("y_made"), sem("z_made")
        ln_stats = [sem(f"ln{i}_stats") for i in (1, 2)]
        ln_mean = [sem(f"ln{i}_mean") for i in (1, 2)]
        ln_var = [sem(f"ln{i}_var") for i in (1, 2)]
        ln_rstd = [sem(f"ln{i}_rstd") for i in (1, 2)]
        zT_copied, xk_scaled, xr_scaled = sem("zT_copied"), sem("xk_scaled"), sem("xr_scaled")
        xk_made, xr_made = sem("xk_made"), sem("xr_made")
        tanh_made, relu_made, sq_made = sem("tanh_made"), sem("relu_made"), sem("sq_made")
        o_made, y2_made, out_made = sem("o_made"), sem("y2_made"), sem("out_made")

        def r_and_k(run, for_r, for_k):
            return (for_r, for_k) if run.exists() else (for_k, for_r)

        taken = {"V": o_made, "WO": y_made, "T": zT_copied, "R": tanh_made, "K": relu_made}

        pieces = [(0, slice(which, which + 1)) for which in range(3)] + [(c, slice(0, 3)) for c in range(1, NC)]
        w_A = [(wrkv_hi[:, c, n], wrkv_lo[:, c, n], wrkv_f[:, c, n], w_rkv[:, c, n]) for c, n in pieces]
        w_rest = [(wo_hi[:], wo_lo[:], wo_f[:], w_o), (wr_hi[:], wr_lo[:], wr_f[:], w_r),
                  (wk_hi[:], wk_lo[:], wk_f[:], w_k), (wv_hi[:], wv_lo[:], wv_f[:], w_v)]
        W_WO, W_R, W_K, W_V = range(4)
        GATE_SCALE = 0.5

        def steps(eng, step, last_block, last_half):
            for s in range(per_batch - 1):
                step(Step(per_batch, s=s, blocks=blocks))
            with eng.Fori(1, batches) as batch:
                for j in range(-1, per_batch - 1):
                    step(Step(per_batch, batch=batch, j=j, blocks=blocks))
            step(Step(per_batch, s=blocks - 1, blocks=blocks))
            last_block(Step(per_batch, s=blocks, blocks=blocks))
            last_half(Step(per_batch, s=blocks + 1, blocks=blocks))

        block = ctx.enter_context(nc.Block())

        @block.sync
        def _(sp):
            def load(piece, loaded):
                _, _, value, source = piece
                sp.dma_start(value, source).then_inc(loaded, 16)

            load(w_A[0], wA_loaded[0])
            for c in range(NC):
                sp.dma_start(x_f[:, c], xT[0, :, c]).then_inc(x_loaded[c], 16)
            load(w_A[1], wA_loaded[1])
            load(w_A[2], wA_loaded[2])
            sp.dma_start(b_sb[:], b_rkv).then_inc(s_small, 16)
            for i, v in enumerate((nu_log, gamma_log, mu_r, mu_k)):
                sp.dma_start(vecs[:, i], v).then_inc(s_small, 16)
            for i in range(3, len(w_A)):
                load(w_A[i], wA_loaded[i])
            sp.dma_start(bo[:], b_o).then_inc(s_bo, 16)
            for i in range(len(w_rest)):
                load(w_rest[i], w_loaded[i])

            def store(s, half):
                for i in range(HT):
                    wait(sp, out_made, s.count(NT, HT * half + i + 1))
                    sp.dma_start(out_rows[s.block() * NT + (HT * half + i)], t[:, HT * half + i])\
                        .then_inc(stored[HT * half + i], 16)

            def load_rows(s, half, user):
                for i in range(HT):
                    tile = HT * half + i
                    wait(sp, y2_made, user.count(NT, tile + 1))
                    sp.dma_start(y[:, y_slot(s, tile)], x_rows[s.block() * NT + tile]).then_inc(y_loaded[tile], 16)

            def load_xT(s):
                wait(sp, r_ready, s.back(1).count(NC, NC))
                for c in range(NC):
                    sp.dma_start(x_f[:, c], xT[s.block(), :, c]).then_inc(x_loaded[c], 16)

            def step(s):
                if s.back(2).exists():
                    store(s.back(2), 1)
                load_rows(s, 1, s.back(2))
                if s.back(-1).exists():
                    load_xT(s.back(-1))
                load_rows(s, 0, s.back(1))
                if s.back(1).exists():
                    store(s.back(1), 0)

            def last_block(s):
                store(s.back(2), 1)
                store(s.back(1), 0)

            def last_half(s):
                store(s.back(2), 1)

            steps(sp, step, last_block, last_half)
            for tile in range(NT):
                sp.wait_ge(stored[tile], 16 * blocks)

        @block.gpsimd
        def _(pool):
            pool.memset(ident[:], 0.0).then_inc(s_id, 1)
            pool.memset(half_pow[:], -0.5).then_inc(s_const, 1)
            pool.wait_ge(s_id, 1)
            pool.affine_select(out=ident[:], in_=ident[:], compare_op=ALU.not_equal, fill=1.0,
                               base=0, pattern=[[-1, P]], channel_multiplier=1).then_inc(s_id, 1)
            pool.wait_ge(s_bo, 16)

            def weight_low(i):
                hi, lo, value, _ = w_rest[i]
                pool.wait_ge(w_hi_made, i + 1)
                pool.tensor_tensor(lo, value, hi, ALU.subtract).then_inc(w_lo_made, 1)

            def att(s, c):
                wait(pool, num_made, s.count(NC, c + 1))
                wait(pool, rec_made, s.count(NC, c + 1))
                pool.tensor_tensor(att_f[:, c], att_f[:, c], gate[:, c % 2], ALU.mult).then_inc(att_made, 1)

            def att_low(s, c):
                wait(pool, att_hi_made, s.count(NC, c + 1))
                pool.tensor_tensor(att_lo[:, c], att_f[:, c], att_hi[:, c], ALU.subtract).then_inc(att_lo_made, 1)

            def inverse_std(s, which, half):
                wait(pool, ln_var[which], s.count(NH, half + 1))
                tiles = slice(HT * half, HT * half + HT)
                pool.tensor_tensor(rstd[:, which, tiles], ve[:, which, tiles], half_pow[:], ALU.pow)\
                    .then_inc(ln_rstd[which], 1)

            def mixed_low(s, half, run):
                for lo, f, hi, hi_made, lo_made in r_and_k(run, (xr_lo, xr_f, xr_hi, xr_hi_made, xr_lo_made),
                                                           (xk_lo, xk_f, xk_hi, xk_hi_made, xk_lo_made)):
                    wait(pool, hi_made, s.count(NH, half + 1))
                    pool.tensor_tensor(lo[:], f[:], hi[:], ALU.subtract).then_inc(lo_made, 1)

            def residual(s, half):
                for i in range(HT):
                    tile = HT * half + i
                    wait(pool, o_made, s.count(NT, tile + 1))
                    pool.tensor_tensor(t[:, tile], t[:, tile], y[:, y_slot(s, tile)], ALU.add).then_inc(y2_made, 1)

            def bias_rows(s):
                for tile in (2, 3, 0, 1):
                    wait(pool, y_loaded[tile], s.count(16, 16))
                    rows = y[:, y_slot(s, tile)]
                    pool.tensor_tensor(rows, rows, bo[:], ALU.add).then_inc(y_biased, 1)

            def step(s):
                s1, s2 = s.back(1), s.back(2)
                first = s.batch is None and s.s == 0
                if s2.exists():
                    residual(s2, 1)
                if s1.exists():
                    inverse_std(s1, 0, 0)
                if s2.exists():
                    inverse_std(s2, 1, 1)
                if s1.exists():
                    inverse_std(s1, 0, 1)
                att(s, 0)
                att_low(s, 0)
                if first:
                    weight_low(W_WO)
                if s1.exists():
                    mixed_low(s1, 0, s)
                att(s, 1)
                att_low(s, 1)
                if first:
                    weight_low(W_R)
                att(s, 2)
                att_low(s, 2)
                if first:
                    weight_low(W_K)
                if s1.exists():
                    mixed_low(s1, 1, s)
                    residual(s1, 0)
                att(s, 3)
                att_low(s, 3)
                if first:
                    weight_low(W_V)
                if s1.exists():
                    inverse_std(s1, 1, 0)
                bias_rows(s)

            def last_block(s):
                s1, s2 = s.back(1), s.back(2)
                inverse_std(s1, 0, 0)
                residual(s2, 1)
                inverse_std(s2, 1, 1)
                mixed_low(s1, 0, s)
                inverse_std(s1, 0, 1)
                mixed_low(s1, 1, s)
                residual(s1, 0)
                inverse_std(s1, 1, 0)

            def last_half(s):
                residual(s.back(2), 1)
                inverse_std(s.back(2), 1, 1)

            steps(pool, step, last_block, last_half)

        @block.scalar
        def _(act):
            def x_high(s):
                for c in range(NC):
                    wait(act, x_loaded[c], s.count(16, 16))
                    wait(act, r_ready, s.back(1).count(NC, NC))
                    act.activation(x_hi[:, c], x_f[:, c], ACT.Copy).then_inc(x_hi_made, 1)

            def weight_A_high(i):
                hi, _, value, _ = w_A[i]
                act.wait_ge(wA_loaded[i], 16)
                act.activation(hi, value, ACT.Copy).then_inc(wA_hi_made, 1)

            def weight_high(i):
                hi, _, value, _ = w_rest[i]
                act.wait_ge(w_loaded[i], 16)
                if i == W_V:
                    act.activation(value, value, ACT.Copy, scale=GATE_SCALE).then_inc(wv_halved, 1)
                    act.wait_ge(wv_halved, 1)
                act.activation(hi, value, ACT.Copy).then_inc(w_hi_made, 1)

            def exp_key(s, c):
                wait(act, k_ready, s.count(NC, c + 1))
                wait(act, scale_made, s.count(NC, c - 1))
                act.activation(key[:, c % 2], bankA[(3 * c) % NBANK][:], ACT.Exp, bias=b_sb[:, 0, c:c + 1])\
                    .then_inc(key_exp, 1)

            def exp_gate(s, c):
                wait(act, r_ready, s.count(NC, c + 1))
                wait(act, att_made, s.count(NC, c - 1))
                act.activation(gate[:, c % 2], bankA[(3 * c + 2) % NBANK][:], ACT.Exp, bias=neg_br[:, c:c + 1],
                               scale=-1.0).then_inc(gate_exp, 1)
                wait(act, gate_exp, s.count(NC, c + 1))
                act.activation(gate[:, c % 2], gate[:, c % 2], ACT.Copy, bias=1.0).then_inc(gate_plus1, 1)

            def att_high(s, c):
                wait(act, att_made, s.count(NC, c + 1))
                act.activation(att_hi[:, c], att_f[:, c], ACT.Copy).then_inc(att_hi_made, 1)

            def copy_zT(s, half):
                wait(act, s_col0, s.count(NH, half + 1))
                for i in range(2):
                    wait(act, ready["T"], s.count(NT, 2 * half + i + 1))
                    src = psum_of("T", 2 * half + i)[:].rearrange("p (c n) -> p c n", c=2)
                    act.activation(zT[:, 2 * i:2 * i + 2, 1:HALF + 1], src, ACT.Copy).then_inc(zT_copied, 1)

            def previous_scaled(s, half, run):
                wait(act, zT_copied, s.count(NT, 2 * half + 2))
                for f, which, made, through in r_and_k(run, (xr_f, 0, xr_scaled, "R"), (xk_f, 1, xk_scaled, "K")):
                    wait(act, ready[through], s.count(NT, 2 * half))
                    for c in range(NC):
                        act.activation(f[:, c], zT[:, c, 0:HALF], ACT.Copy, scale=om_mu[:, which, c:c + 1])\
                            .then_inc(made, 1)

            def mixed_high(s, half, run):
                for hi, f, made, hi_made in r_and_k(run, (xr_hi, xr_f, xr_made, xr_hi_made),
                                                    (xk_hi, xk_f, xk_made, xk_hi_made)):
                    wait(act, made, s.count(NH * NC, NC * half + NC))
                    act.activation(hi[:], f[:], ACT.Copy).then_inc(hi_made, 1)

            def tanh(s, half):
                for i in range(HT):
                    tile = HT * half + i
                    wait(act, ready["R"], s.count(NT, tile + 1))
                    wait(act, stored[tile], s.back(1).count(16, 16))
                    act.activation(t[:, tile], psum_of("R", tile)[:], ACT.Tanh, scale=0.5).then_inc(tanh_made, 1)

            def key_square(s, half):
                for i in range(2):
                    n = 2 * half + i
                    part = slice(2 * i, 2 * i + 2)
                    src = psum_of("K", n)[:].rearrange("p (c n) -> p c n", c=2)
                    wait(act, ready["K"], s.count(NT, n + 1))
                    wait(act, ready["V"], s.count(NT, 2 * half))
                    act.activation(ka_f[:, part], src, ACT.Relu).then_inc(relu_made, 1)
                    wait(act, relu_made, s.count(NT, n + 1))
                    act.activation(ka_hi[:, part], ka_f[:, part], ACT.Square).then_inc(ka_hi_made, 1)
                    wait(act, ka_hi_made, s.count(NT, n + 1))
                    act.activation(ka_f[:, part], ka_f[:, part], ACT.Square).then_inc(sq_made, 1)

            weight_A_high(0)
            x_high(Step(per_batch, s=0, blocks=blocks))
            weight_A_high(1)
            weight_A_high(2)
            act.wait_ge(s_small, 80)
            act.activation(nu[:], vecs[:, 0], ACT.Exp).then_inc(s_actc, 1)
            act.wait_ge(s_actc, 1)
            act.activation(lam[:], nu[:], ACT.Exp, scale=-1.0).then_inc(s_actc, 1)
            weight_A_high(3)
            act.wait_ge(s_dvec, 1)
            act.activation(gamma[:], ngsum[:], ACT.Exp).then_inc(s_actc, 1)
            weight_A_high(4)
            weight_A_high(5)
            act.wait_ge(s_dvec, 3)

            def step(s):
                s1 = s.back(1)
                first = s.batch is None and s.s == 0
                exp_key(s, 0)
                exp_gate(s, 0)
                if first:
                    weight_high(W_WO)
                exp_key(s, 1)
                if s1.exists():
                    copy_zT(s1, 0)
                    previous_scaled(s1, 0, s)
                att_high(s, 0)
                exp_gate(s, 1)
                if first:
                    weight_high(W_R)
                if s1.exists():
                    mixed_high(s1, 0, s)
                exp_key(s, 2)
                exp_gate(s, 2)
                att_high(s, 1)
                if first:
                    weight_high(W_K)
                if s1.exists():
                    copy_zT(s1, 1)
                    tanh(s1, 0)
                    key_square(s1, 0)
                    previous_scaled(s1, 1, s)
                if first:
                    x_high(s.back(-1))
                att_high(s, 2)
                exp_key(s, 3)
                exp_gate(s, 3)
                if first:
                    weight_high(W_V)
                if s1.exists():
                    mixed_high(s1, 1, s)
                if s.back(-1).exists() and not first:
                    x_high(s.back(-1))
                att_high(s, 3)
                if s1.exists():
                    tanh(s1, 1)
                    key_square(s1, 1)

            def last_block(s):
                s1 = s.back(1)
                copy_zT(s1, 0)
                previous_scaled(s1, 0, s)
                mixed_high(s1, 0, s)
                copy_zT(s1, 1)
                key_square(s1, 0)
                tanh(s1, 0)
                previous_scaled(s1, 1, s)
                mixed_high(s1, 1, s)
                key_square(s1, 1)
                tanh(s1, 1)

            def last_half(s):
                pass

            steps(act, step, last_block, last_half)

        @block.vector
        def _(dve):
            dve.memset(zT[:, :, 0:1], 0.0).then_inc(s_col0, 1)
            def weight_A_low(i):
                hi, lo, value, _ = w_A[i]
                dve.wait_ge(wA_hi_made, i + 1)
                dve.tensor_tensor(lo, value, hi, ALU.subtract).then_inc(wA_lo_made, 1)

            def x_low(s):
                for c in range(NC):
                    wait(dve, x_hi_made, s.count(NC, c + 1))
                    dve.tensor_tensor(x_lo[:, c], x_f[:, c], x_hi[:, c], ALU.subtract).then_inc(x_lo_made, 1)

            weight_A_low(0)
            x_low(Step(per_batch, s=0, blocks=blocks))
            weight_A_low(1)
            weight_A_low(2)
            dve.wait_ge(s_small, 80)
            dve.tensor_tensor(ngsum[:], vecs[:, 0], vecs[:, 1], ALU.add).then_inc(s_dvec, 1)
            dve.tensor_scalar(neg_br[:], b_sb[:, 2], -1.0, None, ALU.mult).then_inc(s_dvec, 1)
            dve.tensor_scalar(om_mu[:], vecs[:, 2:4], -1.0, 1.0, ALU.mult, ALU.add).then_inc(s_dvec, 1)
            weight_A_low(3)
            dve.wait_ge(s_actc, 3)
            dve.tensor_scalar(gamma[:], gamma[:], -1.0, None, ALU.add).then_inc(s_dvec, 1)
            weight_A_low(4)
            weight_A_low(5)
            dve.wait_ge(s_dvec, 4)

            def state(s, which, c):
                return 0.0 if s.first_of_batch() else carry[:, which, c:c + 1]

            def denominator(s, c):
                lam_c = lam[:, c:c + 1].to_broadcast([P, TB])
                wait(dve, key_exp, s.count(NC, c + 1))
                wait(dve, u2_saved, s.count(NC, c))
                wait(dve, den_made, s.count(NC, c))
                dve.tensor_tensor_scan(u2[:], lam_c, key[:, c % 2], state(s, 1, c), ALU.mult, ALU.add)\
                    .then_inc(u2_scanned, 1)
                wait(dve, v_ready, s.count(NC, c + 1))
                wait(dve, num_made, s.count(NC, c))
                dve.scalar_tensor_tensor(out=kv[:], in0=bankA[(3 * c + 1) % NBANK][:], scalar=b_sb[:, 1, c:c + 1],
                                         in1=key[:, c % 2], op0=ALU.add, op1=ALU.mult).then_inc(kv_made, 1)
                wait(dve, u2_scanned, s.count(NC, c + 1))
                dve.tensor_copy(carry[:, 1, c:c + 1], u2[:, TB - 1:TB]).then_inc(u2_saved, 1)
                wait(dve, kv_made, s.count(NC, c + 1))
                dve.scalar_tensor_tensor(out=key[:, c % 2], in0=key[:, c % 2], scalar=gamma[:, c:c + 1], in1=u2[:],
                                         op0=ALU.mult, op1=ALU.add).then_inc(den_made, 1)
                wait(dve, den_made, s.count(NC, c + 1))
                wait(dve, gate_plus1, s.count(NC, c + 1))
                dve.scalar_tensor_tensor(out=gate[:, c % 2], in0=key[:, c % 2], scalar=EPS_DEN, in1=gate[:, c % 2],
                                         op0=ALU.add, op1=ALU.mult).then_inc(scale_made, 1)
                wait(dve, scale_made, s.count(NC, c + 1))
                dve.reciprocal(gate[:, c % 2], gate[:, c % 2]).then_inc(rec_made, 1)

            def numerator(s, c):
                lam_c = lam[:, c:c + 1].to_broadcast([P, TB])
                wait(dve, ready["WO"], s.back(1).count(NT, NT))
                wait(dve, kv_made, s.count(NC, c + 1))
                wait(dve, u1_saved, s.count(NC, c))
                dve.tensor_tensor_scan(att_f[:, c], lam_c, kv[:], state(s, 0, c), ALU.mult, ALU.add)\
                    .then_inc(u1_scanned, 1)
                wait(dve, u1_scanned, s.count(NC, c + 1))
                dve.tensor_copy(carry[:, 0, c:c + 1], att_f[:, c, TB - 1:TB]).then_inc(u1_saved, 1)
                wait(dve, u1_saved, s.count(NC, c + 1))
                dve.scalar_tensor_tensor(out=att_f[:, c], in0=kv[:], scalar=gamma[:, c:c + 1], in1=att_f[:, c],
                                         op0=ALU.mult, op1=ALU.add).then_inc(num_made, 1)

            def statistics(s, which, half, rows, made):
                for i in range(HT):
                    tile = HT * half + i
                    wait(dve, made, s.count(NT, tile + 1))
                    dve.bn_stats(st[:, which, tile], rows(tile)).then_inc(ln_stats[which], 1)
                wait(dve, ln_stats[which], s.count(NT, HT * half + HT))
                dve.memset(held[:], 0.0)
                for i in range(HT):
                    tile = HT * half + i
                    dve.bn_aggr(mv[:, which, tile], st[:, which, tile]).then_inc(ln_mean[which], 1)
                wait(dve, ln_mean[which], s.count(NT, HT * half + HT))
                tiles = slice(HT * half, HT * half + HT)
                dve.tensor_scalar(ve[:, which, tiles], mv[:, which, tiles, 1], EPS_LN, None, ALU.add)\
                    .then_inc(ln_var[which], 1)

            def attention_rows(s, half):
                for i in range(HT):
                    tile = HT * half + i
                    rows = y[:, y_slot(s, tile)]
                    wait(dve, ready["WO"], s.count(NT, tile + 1))
                    wait(dve, y_biased, s.count(NT, NT))
                    dve.tensor_tensor(rows, psum_of("WO", tile)[:], rows, ALU.add).then_inc(y_made, 1)
                statistics(s, 0, half, lambda tile: y[:, y_slot(s, tile)], y_made)

            def normalise(s, which, half, rows, done):
                wait(dve, ln_rstd[which], s.count(NH, half + 1))
                for i in range(HT):
                    tile = HT * half + i
                    dve.tensor_scalar(rows(tile), rows(tile), mv[:, which, tile, 0:1], rstd[:, which, tile:tile + 1],
                                      ALU.subtract, ALU.mult).then_inc(done, 1)

            def mix(s, half, next_starts_batch, run):
                for f, which, scaled, made in r_and_k(run, (xr_f, 0, xr_scaled, xr_made),
                                                      (xk_f, 1, xk_scaled, xk_made)):
                    for c in range(NC):
                        wait(dve, scaled, s.count(NH * NC, NC * half + c + 1))
                        dve.scalar_tensor_tensor(out=f[:, c], in0=zT[:, c, 1:HALF + 1],
                                                 scalar=vecs[:, 2 + which, c:c + 1], in1=f[:, c],
                                                 op0=ALU.mult, op1=ALU.add).then_inc(made, 1)
                if next_starts_batch:
                    dve.memset(zT[:, :, 0:1], 0.0).then_inc(s_col0, 1)
                else:
                    dve.tensor_copy(zT[:, :, 0:1], zT[:, :, HALF:HALF + 1]).then_inc(s_col0, 1)

            def key_low(s, half):
                for i in range(2):
                    part = slice(2 * i, 2 * i + 2)
                    wait(dve, sq_made, s.count(NT, 2 * half + i + 1))
                    dve.tensor_tensor(ka_lo[:, part], ka_f[:, part], ka_hi[:, part], ALU.subtract)\
                        .then_inc(ka_lo_made, 1)

            def gated_values(s, half):
                for i in range(HT):
                    tile = HT * half + i
                    wait(dve, ready["V"], s.count(NT, tile + 1))
                    wait(dve, tanh_made, s.count(NT, tile + 1))
                    dve.scalar_tensor_tensor(out=t[:, tile], in0=t[:, tile], scalar=1.0, in1=psum_of("V", tile)[:],
                                             op0=ALU.add, op1=ALU.mult).then_inc(o_made, 1)

            def result_rows(s):
                return lambda tile: t[:, tile]

            def z_rows(s):
                return lambda tile: y[:, y_slot(s, tile)]

            def step(s):
                s1, s2 = s.back(1), s.back(2)
                first = s.batch is None and s.s == 0
                denominator(s, 0)
                if s2.exists():
                    gated_values(s2, 1)
                if s1.exists():
                    attention_rows(s1, 0)
                if s2.exists():
                    statistics(s2, 1, 1, result_rows(s2), y2_made)
                if s1.exists():
                    normalise(s1, 0, 0, z_rows(s1), z_made)
                    attention_rows(s1, 1)
                if s2.exists():
                    normalise(s2, 1, 1, result_rows(s2), out_made)
                if s1.exists():
                    normalise(s1, 0, 1, z_rows(s1), z_made)
                numerator(s, 0)
                if s1.exists():
                    mix(s1, 0, False, s)
                denominator(s, 1)
                numerator(s, 1)
                denominator(s, 2)
                numerator(s, 2)
                if s1.exists():
                    key_low(s1, 0)
                    mix(s1, 1, s.first_of_batch(), s)
                if first:
                    x_low(s.back(-1))
                denominator(s, 3)
                if s1.exists():
                    gated_values(s1, 0)
                if s.back(-1).exists() and not first:
                    x_low(s.back(-1))
                numerator(s, 3)
                if s1.exists():
                    statistics(s1, 1, 0, result_rows(s1), y2_made)
                    normalise(s1, 1, 0, result_rows(s1), out_made)
                    key_low(s1, 1)

            def last_block(s):
                s1, s2 = s.back(1), s.back(2)
                attention_rows(s1, 0)
                gated_values(s2, 1)
                normalise(s1, 0, 0, z_rows(s1), z_made)
                statistics(s2, 1, 1, result_rows(s2), y2_made)
                mix(s1, 0, False, s)
                attention_rows(s1, 1)
                normalise(s2, 1, 1, result_rows(s2), out_made)
                normalise(s1, 0, 1, z_rows(s1), z_made)
                key_low(s1, 0)
                mix(s1, 1, True, s)
                gated_values(s1, 0)
                statistics(s1, 1, 0, result_rows(s1), y2_made)
                normalise(s1, 1, 0, result_rows(s1), out_made)
                key_low(s1, 1)

            def last_half(s):
                s2 = s.back(2)
                gated_values(s2, 1)
                statistics(s2, 1, 1, result_rows(s2), y2_made)
                normalise(s2, 1, 1, result_rows(s2), out_made)

            steps(dve, step, last_block, last_half)

        @block.tensor
        def _(pe):
            def project(s, c, which):
                n = 3 * c + which
                m = n - NBANK
                of = s if m >= 0 else s.back(1)
                m %= 3 * NC
                wait(pe, (key_exp, kv_made, gate_exp)[m % 3], of.count(NC, m // 3 + 1))
                bank = bankA[n % NBANK]
                if s.batch is None and s.s == 0:
                    pe.wait_ge(wA_lo_made, which + 1 if c == 0 else 3 + c)
                for h in range(NC):
                    if n == 0:
                        wait(pe, x_lo_made, s.count(NC, h + 1))
                    w_hi, w_lo = wrkv_hi[:, c, which, h], wrkv_lo[:, c, which, h]
                    pe.matmul(bank[:], w_hi, x_hi[:, h], start=(h == 0), stop=False)
                    pe.matmul(bank[:], w_hi, x_lo[:, h], start=False, stop=False)
                    last = pe.matmul(bank[:], w_lo, x_hi[:, h], start=False, stop=(h == NC - 1))
                last.then_inc((k_ready, v_ready, r_ready)[which], 1)

            def bank_free(s, name, index):
                n = slot_of(name, index) - NBANK
                at = s if n >= 0 else s.back(1)
                what, back, i = SLOTS[n % len(SLOTS)]
                wait(pe, taken[what], at.back(back).count(NT, i + 1))

            def rows_product(s, name, index, a_hi, a_lo, tokens_at, w_hi, w_lo):
                bank = psum_of(name, index)
                for c in range(NC):
                    hi, lo = a_hi[:, c, tokens_at:tokens_at + P], a_lo[:, c, tokens_at:tokens_at + P]
                    pe.matmul(bank[:], hi, w_hi[:, c], start=(c == 0), stop=False)
                    pe.matmul(bank[:], hi, w_lo[:, c], start=False, stop=False)
                    last = pe.matmul(bank[:], lo, w_hi[:, c], start=False, stop=(c == NC - 1))
                last.then_inc(ready[name], 1)

            def attention_out(s, half, run):
                for tile in range(HT * half, HT * half + HT):
                    bank_free(run, "WO", tile)
                    if tile == 0:
                        wait(pe, att_lo_made, s.count(NC, NC))
                    if s.batch is None and s.s == 0:
                        pe.wait_ge(w_lo_made, W_WO + 1)
                    rows_product(s, "WO", tile, att_hi, att_lo, tile * P, wo_hi, wo_lo)

            def transposes(s, half, run):
                for i in range(2):
                    n = 2 * half + i
                    bank_free(run, "T", n)
                    wait(pe, z_made, s.count(NT, HT * half + HT))
                    if s.batch is None and s.s == 0:
                        pe.wait_ge(s_id, 2)
                    for c in range(2):
                        for tile in range(HT):
                            at = c * HALF + tile * P
                            chunk = 2 * i + c
                            rows = y[:, y_slot(s, HT * half + tile), chunk * P:(chunk + 1) * P]
                            last = pe.transpose(psum_of("T", n)[:, at:at + P], rows, ident[:])
                    last.then_inc(ready["T"], 1)

            def receptance(s, half, run):
                for i in range(HT):
                    bank_free(run, "R", HT * half + i)
                    wait(pe, xr_lo_made, s.count(NH, half + 1))
                    if s.batch is None and s.s == 0:
                        pe.wait_ge(w_lo_made, W_R + 1)
                    rows_product(s, "R", HT * half + i, xr_hi, xr_lo, i * P, wr_hi, wr_lo)

            def keys(s, half, run):
                for i in range(2):
                    n = 2 * half + i
                    bank_free(run, "K", n)
                    wait(pe, xk_lo_made, s.count(NH, half + 1))
                    if s.batch is None and s.s == 0:
                        pe.wait_ge(w_lo_made, W_K + 1)
                    for d in range(2):
                        dst = psum_of("K", n)[:, d * HALF:(d + 1) * HALF]
                        cols = slice((2 * i + d) * P, (2 * i + d + 1) * P)
                        for c in range(NC):
                            pe.matmul(dst, wk_hi[:, c, cols], xk_hi[:, c], start=(c == 0), stop=False)
                            pe.matmul(dst, wk_hi[:, c, cols], xk_lo[:, c], start=False, stop=False)
                            last = pe.matmul(dst, wk_lo[:, c, cols], xk_hi[:, c], start=False, stop=(c == NC - 1))
                    last.then_inc(ready["K"], 1)

            def values(s, half, run):
                for i in range(HT):
                    bank_free(run, "V", HT * half + i)
                    wait(pe, ka_lo_made, s.count(NT, 2 * half + 2))
                    if s.batch is None and s.s == 0:
                        pe.wait_ge(w_lo_made, W_V + 1)
                    rows_product(s, "V", HT * half + i, ka_hi, ka_lo, i * P, wv_hi, wv_lo)

            def step(s):
                s1, s2 = s.back(1), s.back(2)
                for which in range(3):
                    project(s, 0, which)
                if s2.exists():
                    values(s2, 1, s)
                if s1.exists():
                    attention_out(s1, 0, s)
                    attention_out(s1, 1, s)
                project(s, 1, 0)
                if s1.exists():
                    transposes(s1, 0, s)
                project(s, 1, 1)
                project(s, 1, 2)
                for which in range(3):
                    project(s, 2, which)
                if s1.exists():
                    transposes(s1, 1, s)
                    receptance(s1, 0, s)
                    keys(s1, 0, s)
                for which in range(3):
                    project(s, 3, which)
                if s1.exists():
                    values(s1, 0, s)
                    receptance(s1, 1, s)
                    keys(s1, 1, s)

            def last_block(s):
                s1, s2 = s.back(1), s.back(2)
                attention_out(s1, 0, s)
                values(s2, 1, s)
                transposes(s1, 0, s)
                attention_out(s1, 1, s)
                transposes(s1, 1, s)
                keys(s1, 0, s)
                receptance(s1, 0, s)
                values(s1, 0, s)
                keys(s1, 1, s)
                receptance(s1, 1, s)

            def last_half(s):
                values(s.back(2), 1, s)

            steps(pe, step, last_block, last_half)


def kernel(**inputs):
    import numpy as np
    import concourse.bacc as bacc
    from concourse.bass_utils import run_bass_kernel_spmd

    x = np.asarray(inputs["L0_attn_inputs"])
    B, L, Hx = x.shape
    tokens = B * L
    rows = x.reshape(tokens, Hx)
    xT = rows.reshape(tokens // TB, TB, NC, P).transpose(0, 3, 2, 1)
    w = np.asarray(inputs["L0_attn_W_rkv"]).reshape(NC, P, 3, NC, P)[:, :, [1, 2, 0]].transpose(1, 3, 2, 0, 4)

    def by_input(m):
        return np.asarray(m).reshape(NC, P, H).transpose(1, 0, 2)

    def by_channel(v):
        return np.asarray(v).reshape(NC, P).T

    arrays = {
        "xT": xT, "x": rows, "w_rkv": w,
        "w_o": by_input(inputs["L0_attn_W_o"]),
        "w_r": by_input(np.asarray(inputs["L0_ffn_W_r"]).T),
        "w_k": by_input(np.asarray(inputs["L0_ffn_W_k"]).T),
        "w_v": by_input(np.asarray(inputs["L0_ffn_W_v"]).T),
        "b_rkv": np.asarray(inputs["L0_attn_b_rkv"]).reshape(3, NC, P)[[1, 2, 0]].transpose(2, 0, 1),
        "b_o": np.broadcast_to(np.asarray(inputs["L0_attn_b_o"]), (P, H)),
        "nu_log": by_channel(inputs["L0_attn_nu_log"]),
        "gamma_log": by_channel(inputs["L0_attn_gamma_log"]),
        "mu_r": by_channel(inputs["L0_ffn_mu_r"]),
        "mu_k": by_channel(inputs["L0_ffn_mu_k"]),
    }
    nc = bacc.Bacc("TRN2", target_bir_lowering=False, num_devices=1)
    sent, aps = {}, []
    for name, a in arrays.items():
        a = np.ascontiguousarray(a)
        sent[f"in_{name}"] = a
        aps.append(nc.dram_tensor(f"in_{name}", a.shape, mybir.dt.from_np(a.dtype), kind="ExternalInput").ap())
    out = nc.dram_tensor("out", (tokens, Hx), F32, kind="ExternalOutput").ap()
    program(nc, *aps, out, L)
    r = run_bass_kernel_spmd(nc, [sent], core_ids=[0])
    return r.results[0]["out"].reshape(B, L, Hx)
```
